# Optimizing a Trainium2 kernel written in Bass

```python
import numpy as np
import jax
import jax.numpy as jnp

def _softmax(x, axis=-1):
    return jax.nn.softmax(x, axis=axis)

def _gelu(x):
    return jax.nn.gelu(x, approximate=True)

def _silu(x):
    return jax.nn.silu(x)

def _sigmoid(x):
    return jax.nn.sigmoid(x)

def _layernorm(x, axis=-1, eps=1e-05):
    m = jnp.mean(x, axis=axis, keepdims=True)
    v = jnp.var(x, axis=axis, keepdims=True)
    return (x - m) / jnp.sqrt(v + eps)

def _scatter_add(tgt, idx, src, axis=0):
    return tgt.at[idx].add(src)

def _segment_sum(src, seg, n):
    return jax.ops.segment_sum(src, seg, n)
kernel_name = 'mk_audio_tower_d1_tok_aud1d1024_r4_7cfa3a'

def setup_inputs(seed: int=0):
    np.random.seed(seed)
    _w = jnp.asarray

    def _rec_inputs():
        import jax
        import jax.numpy as jnp
        _rk = jax.random.key(seed)
        x = -9.80646e-05 + 1.00041 * jax.random.normal(jax.random.fold_in(_rk, 1), (64, 2048), jnp.float32)
        return x
    x = _rec_inputs()

    def _L0_tok_setup():
        import jax, jax.numpy as jnp
        import numpy as np
        TOKEN_LEN = 16
        key = jax.random.key(seed)
        ks = jax.random.split(key, 7)
        B, L = (64, 2048)
        D_IN, D_MID, D_OUT = (2 * TOKEN_LEN, 1024, 256)
        s_in = 1.0 / np.sqrt(D_IN)
        s_mid = 1.0 / np.sqrt(D_MID)
        return {'x': jax.random.normal(ks[0], (B, L), dtype=jnp.float32), 'W_h': jax.random.normal(ks[1], (D_IN, D_MID), dtype=jnp.float32) * s_in, 'b_h': jax.random.normal(ks[2], (D_MID,), dtype=jnp.float32) * s_in, 'W_o': jax.random.normal(ks[3], (D_MID, D_OUT), dtype=jnp.float32) * s_mid, 'b_o': jax.random.normal(ks[4], (D_OUT,), dtype=jnp.float32) * s_mid, 'W_r': jax.random.normal(ks[5], (D_IN, D_OUT), dtype=jnp.float32) * s_in, 'b_r': jax.random.normal(ks[6], (D_OUT,), dtype=jnp.float32) * s_in}
    _L0_tok_all = _L0_tok_setup()
    _L0_tok_in = {k: v for k, v in _L0_tok_all.items() if k in ('W_h', 'b_h', 'W_o', 'b_o', 'W_r', 'b_r')}
    del _L0_tok_all

    def _L0_attn_setup():
        import jax, jax.numpy as jnp
        import numpy as np
        NUM_HEADS = 16
        key = jax.random.key(seed)
        x = jax.random.normal(key, (4, 512, 256), dtype=jnp.float32)
        return {'x': x}
    _L0_attn_all = _L0_attn_setup()
    _L0_attn_in = {k: v for k, v in _L0_attn_all.items() if k in ()}
    del _L0_attn_all

    def _L0_ffn_setup():
        import jax, jax.numpy as jnp
        import numpy as np
        DIM = 256
        DEPTH = 2
        HEADS = 8
        DIM_HEAD = 64
        WINDOW = 128
        INNER = HEADS * DIM_HEAD
        HID = int(DIM * 4 * 2 / 3)
        B, N = (2, 2048)
        QK_SCALE = 8.0

        def shift_token(t):
            t1, t2 = jnp.split(t, 2, axis=-1)
            t2 = jnp.pad(t2, ((0, 0), (1, 0), (0, 0)))[:, :-1]
            return jnp.concatenate([t1, t2], axis=-1)

        def l2norm(t):
            return t / jnp.clip(jnp.linalg.norm(t, axis=-1, keepdims=True), 1e-12)

        def rotate_half(x):
            x1, x2 = jnp.split(x, 2, axis=-1)
            return jnp.concatenate([-x2, x1], axis=-1)

        def rotary_xpos(q, k):
            n = q.shape[-2]
            half_idx = jnp.arange(0, DIM_HEAD, 2, dtype=jnp.float32)
            inv_freq = 1.0 / 10000.0 ** (half_idx / DIM_HEAD)
            t = jnp.arange(n, dtype=jnp.float32)
            freqs = t[:, None] * inv_freq[None, :]
            freqs = jnp.concatenate([freqs, freqs], axis=-1)
            base = (half_idx + 0.4 * DIM_HEAD) / (1.4 * DIM_HEAD)
            power = (t - n // 2) / float(WINDOW // 2)
            scale = base[None, :] ** power[:, None]
            scale = jnp.concatenate([scale, scale], axis=-1)
            cos, sin = (jnp.cos(freqs), jnp.sin(freqs))
            q = q * cos * scale + rotate_half(q) * sin * scale
            k = k * cos / scale + rotate_half(k) * sin / scale
            return (q, k)

        def local_attention(q, k, v):
            b, h, n, d = q.shape
            w = n // WINDOW
            bq = q.reshape(b, h, w, WINDOW, d) * QK_SCALE
            bk = k.reshape(b, h, w, WINDOW, d)
            bv = v.reshape(b, h, w, WINDOW, d)

            def look_around(t):
                p = jnp.pad(t, ((0, 0), (0, 0), (1, 0), (0, 0), (0, 0)))
                return jnp.concatenate([p[:, :, :w], p[:, :, 1:]], axis=3)
            bk, bv = (look_around(bk), look_around(bv))
            bt = jnp.arange(n).reshape(w, WINDOW)
            btp = jnp.pad(bt, ((1, 0), (0, 0)), constant_values=-1)
            btk = jnp.concatenate([btp[:w], btp[1:]], axis=1)
            sim = jnp.einsum('bhwid,bhwjd->bhwij', bq, bk)
            i = bt[:, :, None]
            j = btk[:, None, :]
            mask = (i < j) | (i > j + WINDOW) | (j == -1)
            sim = jnp.where(mask, -jnp.finfo(sim.dtype).max, sim)
            attn = jax.nn.softmax(sim, axis=-1)
            out = jnp.einsum('bhwij,bhwjd->bhwid', attn, bv)
            return out.reshape(b, h, n, d)

        def _layer(x, wqkv, qs, ksc, wo, lg, lb, w1, b1, w2, b2):
            b, n, _ = x.shape
            h = shift_token(x)
            qkv = h @ wqkv
            q, k, v = jnp.split(qkv, 3, axis=-1)
            to_heads = lambda t: t.reshape(b, n, HEADS, DIM_HEAD).transpose(0, 2, 1, 3)
            q, k, v = (to_heads(q), to_heads(k), to_heads(v))
            q = l2norm(q) * qs
            k = l2norm(k) * ksc
            q, k = rotary_xpos(q, k)
            o = local_attention(q, k, v)
            o = o.transpose(0, 2, 1, 3).reshape(b, n, INNER)
            x = x + o @ wo
            h = shift_token(x)
            mu = h.mean(-1, keepdims=True)
            var = h.var(-1, keepdims=True)
            h = (h - mu) / jnp.sqrt(var + 1e-05) * lg + lb
            h = h @ w1 + b1
            a, g = jnp.split(h, 2, axis=-1)
            h = a * jax.nn.gelu(g, approximate=False)
            x = x + h @ w2 + b2
            return x
        key = jax.random.key(seed)
        ks = jax.random.split(key, 6)
        return {'x': jax.random.normal(ks[0], (B, N, DIM), jnp.float32), 'wqkv': jax.random.normal(ks[1], (DEPTH, DIM, 3 * INNER), jnp.float32) * 0.02, 'q_scale': jnp.ones((DEPTH, DIM_HEAD), jnp.float32), 'k_scale': jnp.ones((DEPTH, DIM_HEAD), jnp.float32), 'wo': jax.random.normal(ks[2], (DEPTH, INNER, DIM), jnp.float32) * 0.02, 'ln_g': jnp.ones((DEPTH, DIM), jnp.float32), 'ln_b': jnp.zeros((DEPTH, DIM), jnp.float32), 'w1': jax.random.normal(ks[3], (DEPTH, DIM, 2 * HID), jnp.float32) * 0.02, 'b1': jnp.zeros((DEPTH, 2 * HID), jnp.float32), 'w2': jax.random.normal(ks[4], (DEPTH, HID, DIM), jnp.float32) * 0.02, 'b2': jnp.zeros((DEPTH, DIM), jnp.float32)}
    _L0_ffn_all = _L0_ffn_setup()
    _L0_ffn_in = {k: v for k, v in _L0_ffn_all.items() if k in ('wqkv', 'q_scale', 'k_scale', 'wo', 'ln_g', 'ln_b', 'w1', 'b1', 'w2', 'b2')}
    del _L0_ffn_all
    return {'x': x, 'L0_tok_W_h': _L0_tok_in['W_h'], 'L0_tok_b_h': _L0_tok_in['b_h'], 'L0_tok_W_o': _L0_tok_in['W_o'], 'L0_tok_b_o': _L0_tok_in['b_o'], 'L0_tok_W_r': _L0_tok_in['W_r'], 'L0_tok_b_r': _L0_tok_in['b_r'], 'L0_ffn_wqkv': _L0_ffn_in['wqkv'], 'L0_ffn_q_scale': _L0_ffn_in['q_scale'], 'L0_ffn_k_scale': _L0_ffn_in['k_scale'], 'L0_ffn_wo': _L0_ffn_in['wo'], 'L0_ffn_ln_g': _L0_ffn_in['ln_g'], 'L0_ffn_ln_b': _L0_ffn_in['ln_b'], 'L0_ffn_w1': _L0_ffn_in['w1'], 'L0_ffn_b1': _L0_ffn_in['b1'], 'L0_ffn_w2': _L0_ffn_in['w2'], 'L0_ffn_b2': _L0_ffn_in['b2']}

def reference(x, L0_tok_W_h, L0_tok_b_h, L0_tok_W_o, L0_tok_b_o, L0_tok_W_r, L0_tok_b_r, L0_ffn_wqkv, L0_ffn_q_scale, L0_ffn_k_scale, L0_ffn_wo, L0_ffn_ln_g, L0_ffn_ln_b, L0_ffn_w1, L0_ffn_b1, L0_ffn_w2, L0_ffn_b2):
    import jax
    import jax.numpy as jnp

    def _L0_tok_ref(x, W_h, b_h, W_o, b_o, W_r, b_r):
        import jax, jax.numpy as jnp
        import numpy as np
        TOKEN_LEN = 16
        mask = jnp.ones_like(x)
        L = x.shape[-1]
        pad = -L % TOKEN_LEN
        x = jnp.pad(x, ((0, 0), (pad, 0)))
        mask = jnp.pad(mask, ((0, 0), (pad, 0)))
        B = x.shape[0]
        n = x.shape[-1] // TOKEN_LEN
        xp = x.reshape(B, n, TOKEN_LEN)
        mp = mask.reshape(B, n, TOKEN_LEN)
        xm = jnp.concatenate([xp, mp], axis=-1)
        hid = jax.nn.silu(jnp.einsum('bnd,dm->bnm', xm, W_h) + b_h)
        out = jnp.einsum('bnm,mh->bnh', hid, W_o) + b_o
        res = jnp.einsum('bnd,dh->bnh', xm, W_r) + b_r
        return out + res

    def _L0_attn_ref(x):
        import jax, jax.numpy as jnp
        import numpy as np
        NUM_HEADS = 16
        B, T, D = x.shape
        H = NUM_HEADS
        hd = D // H
        xh = x.reshape(B, T, H, hd)
        x_centered = xh - jnp.mean(xh, axis=1, keepdims=True)
        corr = jnp.einsum('bthd,bThd->bhtT', x_centered, x_centered)
        corr = jax.nn.softmax(corr, axis=-1)
        out = jnp.einsum('bhtT,bThd->bthd', corr, xh)
        return out.reshape(B, T, D)

    def _L0_ffn_ref(x, wqkv, q_scale, k_scale, wo, ln_g, ln_b, w1, b1, w2, b2):
        import jax, jax.numpy as jnp
        import numpy as np
        DIM = 256
        DEPTH = 2
        HEADS = 8
        DIM_HEAD = 64
        WINDOW = 128
        INNER = HEADS * DIM_HEAD
        HID = int(DIM * 4 * 2 / 3)
        B, N = (2, 2048)
        QK_SCALE = 8.0

        def shift_token(t):
            t1, t2 = jnp.split(t, 2, axis=-1)
            t2 = jnp.pad(t2, ((0, 0), (1, 0), (0, 0)))[:, :-1]
            return jnp.concatenate([t1, t2], axis=-1)

        def l2norm(t):
            return t / jnp.clip(jnp.linalg.norm(t, axis=-1, keepdims=True), 1e-12)

        def rotate_half(x):
            x1, x2 = jnp.split(x, 2, axis=-1)
            return jnp.concatenate([-x2, x1], axis=-1)

        def rotary_xpos(q, k):
            n = q.shape[-2]
            half_idx = jnp.arange(0, DIM_HEAD, 2, dtype=jnp.float32)
            inv_freq = 1.0 / 10000.0 ** (half_idx / DIM_HEAD)
            t = jnp.arange(n, dtype=jnp.float32)
            freqs = t[:, None] * inv_freq[None, :]
            freqs = jnp.concatenate([freqs, freqs], axis=-1)
            base = (half_idx + 0.4 * DIM_HEAD) / (1.4 * DIM_HEAD)
            power = (t - n // 2) / float(WINDOW // 2)
            scale = base[None, :] ** power[:, None]
            scale = jnp.concatenate([scale, scale], axis=-1)
            cos, sin = (jnp.cos(freqs), jnp.sin(freqs))
            q = q * cos * scale + rotate_half(q) * sin * scale
            k = k * cos / scale + rotate_half(k) * sin / scale
            return (q, k)

        def local_attention(q, k, v):
            b, h, n, d = q.shape
            w = n // WINDOW
            bq = q.reshape(b, h, w, WINDOW, d) * QK_SCALE
            bk = k.reshape(b, h, w, WINDOW, d)
            bv = v.reshape(b, h, w, WINDOW, d)

            def look_around(t):
                p = jnp.pad(t, ((0, 0), (0, 0), (1, 0), (0, 0), (0, 0)))
                return jnp.concatenate([p[:, :, :w], p[:, :, 1:]], axis=3)
            bk, bv = (look_around(bk), look_around(bv))
            bt = jnp.arange(n).reshape(w, WINDOW)
            btp = jnp.pad(bt, ((1, 0), (0, 0)), constant_values=-1)
            btk = jnp.concatenate([btp[:w], btp[1:]], axis=1)
            sim = jnp.einsum('bhwid,bhwjd->bhwij', bq, bk)
            i = bt[:, :, None]
            j = btk[:, None, :]
            mask = (i < j) | (i > j + WINDOW) | (j == -1)
            sim = jnp.where(mask, -jnp.finfo(sim.dtype).max, sim)
            attn = jax.nn.softmax(sim, axis=-1)
            out = jnp.einsum('bhwij,bhwjd->bhwid', attn, bv)
            return out.reshape(b, h, n, d)

        def _layer(x, wqkv, qs, ksc, wo, lg, lb, w1, b1, w2, b2):
            b, n, _ = x.shape
            h = shift_token(x)
            qkv = h @ wqkv
            q, k, v = jnp.split(qkv, 3, axis=-1)
            to_heads = lambda t: t.reshape(b, n, HEADS, DIM_HEAD).transpose(0, 2, 1, 3)
            q, k, v = (to_heads(q), to_heads(k), to_heads(v))
            q = l2norm(q) * qs
            k = l2norm(k) * ksc
            q, k = rotary_xpos(q, k)
            o = local_attention(q, k, v)
            o = o.transpose(0, 2, 1, 3).reshape(b, n, INNER)
            x = x + o @ wo
            h = shift_token(x)
            mu = h.mean(-1, keepdims=True)
            var = h.var(-1, keepdims=True)
            h = (h - mu) / jnp.sqrt(var + 1e-05) * lg + lb
            h = h @ w1 + b1
            a, g = jnp.split(h, 2, axis=-1)
            h = a * jax.nn.gelu(g, approximate=False)
            x = x + h @ w2 + b2
            return x
        for l in range(DEPTH):
            x = _layer(x, wqkv[l], q_scale[l], k_scale[l], wo[l], ln_g[l], ln_b[l], w1[l], b1[l], w2[l], b2[l])
        return x
    h = _L0_tok_ref(x, L0_tok_W_h, L0_tok_b_h, L0_tok_W_o, L0_tok_b_o, L0_tok_W_r, L0_tok_b_r)
    h = h + _L0_attn_ref(_layernorm(h, axis=-1))
    h = h + _L0_ffn_ref(_layernorm(h, axis=-1), L0_ffn_wqkv, L0_ffn_q_scale, L0_ffn_k_scale, L0_ffn_wo, L0_ffn_ln_g, L0_ffn_ln_b, L0_ffn_w1, L0_ffn_b1, L0_ffn_w2, L0_ffn_b2)
    return h

_drawn_inputs = setup_inputs


def setup_inputs(seed=0):
    import zlib

    import numpy as np

    out = dict(_drawn_inputs(seed))
    spreads = {'L0_ffn_q_scale': (1.0, 0.6),
     'L0_ffn_k_scale': (1.0, 0.6),
     'L0_ffn_ln_g': (1.0, 0.6),
     'L0_ffn_ln_b': (0.0, 0.8),
     'L0_ffn_b1': (0.0, 0.8),
     'L0_ffn_b2': (0.0, 0.408)}
    factors = {'L0_ffn_w1': 3.591, 'L0_ffn_w2': 3.457}
    for name, (base, spread) in spreads.items():
        noise = np.random.default_rng([zlib.crc32(name.encode()), seed]).standard_normal(out[name].shape)
        drawn = base * np.exp(spread * noise) if base else spread * noise
        out[name] = jnp.asarray(drawn.astype(out[name].dtype))
    for name, factor in factors.items():
        out[name] = (out[name] * factor).astype(out[name].dtype)
    return out
```

```python
from contextlib import ExitStack

import numpy as np

import concourse.bass as bass
from concourse import mybir

F32 = mybir.dt.float32
F32R = mybir.dt.float32r
BF16 = mybir.dt.bfloat16
ALU = mybir.AluOpType
ACT = mybir.ActivationFunctionType
AX_X = mybir.AxisListType.X

P = 128
ROWS, LENGTH = 64, 2048
PATCH = 16
TOKENS = LENGTH // PATCH
D = 256
KD = D // P
MID = 1024
KM = MID // P
IH, IHD = 16, 16
HEADS, HD = 8, 64
INNER = HEADS * HD
KI = INNER // P
HID = int(D * 4 * 2 / 3)
KH = -(-HID // P)
HTAIL = HID - (KH - 1) * P
HPAD = KH * P
BIAS_ROW = 64
DEPTH = 2
GROUP = 4
GROUPS = ROWS // GROUP
GT = GROUP * TOKENS
STACK = 3 * PATCH + 2 * (PATCH + 2)
EPS = 1e-5
MASKED = -1e30


def need(eng, sem, n):
    if not isinstance(n, int) or n > 0:
        eng.wait_ge(sem, n)


def take_wait(dve, scratch):
    dve.memset(scratch, 0.0)


def run_steps(eng, count, depth, body, unroll=2):
    head = -(-(depth + 2) // unroll) * unroll

    def peeled(t):
        u = t % unroll
        body(t, (t - u) // 2, u, lambda lag: 0 <= t - lag < count)

    for t in range(head):
        peeled(t)
    with eng.Fori(head // unroll, count // unroll) as i:
        for u in range(unroll):
            body(unroll * i + u, unroll // 2 * i, u, lambda lag: True)
    for t in range(count, count + depth):
        peeled(t)


def at_lag(j, u, lag):
    return j + (u - lag) // 2, (u - lag) % 2


class Memory:

    def __init__(self, nc, ctx, stage):
        self.nc, self.ctx, self.stage, self.sems = nc, ctx, stage, []

    def sb(self, name, shape, dt=F32):
        return self.ctx.enter_context(self.nc.sbuf_tensor(f"{self.stage}_{name}", shape, dt))

    def psum(self, name, shape, dt=F32):
        return self.ctx.enter_context(self.nc.psum_tensor(f"{self.stage}_{name}", shape, dt))

    def sem(self, name):
        s = self.nc.alloc_semaphore(f"{self.stage}_{name}")
        self.sems.append(s)
        return s

    def end(self):
        self.nc.clear_and_free_semaphores(self.sems)
        self.nc.all_engine_barrier()


def constants(nc, m):
    c = {
        "ident": m.sb("ident", [P, P]),
        "ident_b": m.sb("ident_b", [P, P], BF16),
        "shift": m.sb("shift", [P, P]),
        "mean": m.sb("mean", [P, P]),
        "causal": m.sb("causal", [P, 4, P], BF16),
        "sel": m.sb("sel", [3 * IH, IH, P], BF16),
        "banks": m.psum("banks", [P, 8, 512]),
        "neg_half": m.sb("neg_half", [P, IH]),
    }
    cleared, made = m.sem("const_cleared"), m.sem("const_made")
    with nc.Block() as block:

        @block.gpsimd
        def _(pool):
            for name, value in (("ident", 0.0), ("ident_b", 0.0), ("shift", 0.0), ("mean", 1.0 / TOKENS),
                                ("causal", 0.0), ("sel", 0.0), ("neg_half", -0.5)):
                pool.memset(c[name][:], value).then_inc(cleared, 1)
            pool.wait_ge(cleared, 7)
            for name in ("ident", "ident_b"):
                pool.affine_select(out=c[name][:], in_=c[name][:], compare_op=ALU.not_equal, fill=1.0, base=0,
                                   pattern=[[-1, P]], channel_multiplier=1).then_inc(made, 1)
            pool.affine_select(out=c["shift"][:], in_=c["shift"][:], compare_op=ALU.not_equal, fill=1.0, base=-1,
                               pattern=[[1, P]], channel_multiplier=-1).then_inc(made, 1)
            pool.affine_select(out=c["causal"][:], in_=c["causal"][:], compare_op=ALU.is_ge, fill=MASKED, base=0,
                               pattern=[[0, 4], [-1, P]], channel_multiplier=1).then_inc(made, 1)
            for part in range(3):
                pool.affine_select(out=c["sel"][:], in_=c["sel"][:], compare_op=ALU.not_equal, fill=-1.0,
                                   base=-part * IH, pattern=[[-1, IH], [0, P]],
                                   channel_multiplier=1).then_inc(made, 1)
                pool.wait_ge(made, 5 + part)
    m.end()
    return c


def split(dve, hi, lo, src, count, n):
    dve.tensor_copy(hi, src).then_inc(count, 1)
    dve.wait_ge(count, n + 1)
    dve.tensor_tensor(lo, src, hi.bitcast(F32), ALU.subtract).then_inc(count, 1)


def tokenizer(nc, c, x, W_h, b_h, W_o, b_o, W_r, b_r, h_out):
    NW = MID + D
    ROWS_W = 2 * PATCH + 2
    with ExitStack() as ctx:
        m = Memory(nc, ctx, "tok")
        x_tok = m.sb("x_tok", [P, 2, GROUP, PATCH])
        x_stack = m.sb("x_stack", [P, 2, GROUP, STACK], F32R)
        w_in = m.sb("w_in", [ROWS_W, NW])
        w_in_hi = m.sb("w_in_hi", [ROWS_W, NW], F32R)
        w_in_lo = m.sb("w_in_lo", [ROWS_W, NW], F32R)
        w_stack = m.sb("w_stack", [STACK, NW], F32R)
        wo = m.sb("wo_tok", [P, KM, D])
        wo_hi = m.sb("wo_tok_hi", [P, KM, D], F32R)
        wo_lo = m.sb("wo_tok_lo", [P, KM, D], F32R)
        xT = m.sb("xT", [STACK, 2, GT], F32R)
        hid = m.sb("hid", [P, 2, GT])
        hid_hi = m.sb("hid_hi", [P, 2, KM, GT], F32R)
        hid_lo = m.sb("hid_lo", [P, 2, KM, GT], F32R)
        h_sb = m.sb("h_sb", [P, 2, GROUP, D])
        banks = c["banks"]
        ps_T = banks[:, 0]
        ps_hid = banks[:, 1:5]
        ps_out = banks[:, 5:7]

        w_clear, ones_set = m.sem("w_clear"), m.sem("ones_set")
        x_in = [m.sem("x_in0"), m.sem("x_in1")]
        win_in, wo_in, win_split, wo_split, stacked = [
            m.sem(n) for n in ("win_in", "wo_in", "win_split", "wo_split", "stacked")]
        x_hi, x_lo, xT_ps, xT_ready, xT_used = [m.sem(n) for n in ("x_hi", "x_lo", "xT_ps", "xT_ready", "xT_used")]
        hid_ps, silu_done, hi_done, lo_done = [m.sem(n) for n in ("hid_ps", "silu_done", "hi_done", "lo_done")]
        out_ps, out_sb = m.sem("out_ps"), m.sem("out_sb")
        stored = [m.sem("h_stored0"), m.sem("h_stored1")]

        with nc.Block() as block:

            @block.sync
            def _(sp):
                sp.wait_ge(w_clear, 1)
                sp.dma_start(w_in[0:2 * PATCH, 0:MID], W_h).then_inc(win_in, 16)
                sp.dma_start(w_in[0:2 * PATCH, MID:NW], W_r).then_inc(win_in, 16)
                sp.dma_start(w_in[2 * PATCH:2 * PATCH + 1, 0:MID], b_h.rearrange("(a n) -> a n", a=1)).then_inc(win_in, 16)
                sp.dma_start(w_in[2 * PATCH:2 * PATCH + 1, MID:NW], b_r.rearrange("(a n) -> a n", a=1)).then_inc(win_in, 16)
                sp.dma_start(w_in[2 * PATCH + 1:ROWS_W, MID:NW], b_o.rearrange("(a n) -> a n", a=1)).then_inc(win_in, 16)
                sp.dma_start(wo[:], W_o.rearrange("(k p) n -> p k n", p=P)).then_inc(wo_in, 16)
                sp.wait_ge(win_split, 2)
                one = 3 * PATCH
                for row, src in ((0, w_in_hi[0:PATCH]), (PATCH, w_in_lo[0:PATCH]), (2 * PATCH, w_in_hi[0:PATCH]),
                                 (one, w_in_hi[PATCH:ROWS_W]), (one + PATCH + 2, w_in_lo[PATCH:ROWS_W])):
                    sp.dma_start(w_stack[row:row + src.shape[0], :].bitcast(F32), src.bitcast(F32)).then_inc(stacked, 16)

                def body(t, j, u, on):
                    if on(0):
                        need(sp, x_lo, t - 1)
                        sp.dma_start(x_tok[:, u], x[bass.ds(GROUP * t, GROUP)].rearrange("b (n d) -> n b d", d=PATCH)
                                     ).then_inc(x_in[u], 16)
                    if on(2):
                        _, slot = at_lag(j, u, 2)
                        need(sp, out_sb, 2 * (t - 2) + 2)
                        sp.dma_start(h_out[bass.ds(GROUP * (t - 2), GROUP)].rearrange("b n f -> n b f"),
                                     h_sb[:, slot]).then_inc(stored[slot], 16)

                run_steps(sp, GROUPS, 2, body)
                for s in stored:
                    sp.wait_ge(s, 16 * GROUPS // 2)

            @block.gpsimd
            def _(pool):
                pool.memset(w_in[:], 0.0).then_inc(w_clear, 1)
                pool.memset(x_stack[:].bitcast(F32), 1.0).then_inc(ones_set, 1)

            @block.scalar
            def _(act):
                def body(t, j, u, on):
                    half, slot = at_lag(j, u, 2)
                    for k in range(KM):
                        if on(1):
                            n = KM * (t - 1) + k
                            need(act, hid_ps, n + 1)
                            need(act, lo_done, n - 1)
                            act.activation(hid[:, k % 2], ps_hid[:, k % 4], ACT.Silu).then_inc(silu_done, 1)
                        if on(2) and k == 5:
                            evacuate(act, t, half, slot, 0)
                    if on(0):
                        need(act, xT_ps, t + 1)
                        need(act, xT_used, t - 1)
                        act.activation(xT[:, u], ps_T[0:STACK, :], ACT.Copy).then_inc(xT_ready, 1)
                    if on(2):
                        evacuate(act, t, half, slot, 1)

                def evacuate(act, t, half, slot, pair):
                    need(act, out_ps, 2 * (t - 2) + pair + 1)
                    need(act, stored[slot], 16 * half)
                    act.activation(h_sb[:, slot, 2 * pair:2 * pair + 2], ps_out[:, pair], ACT.Copy).then_inc(out_sb, 1)

                run_steps(act, GROUPS, 2, body)

            @block.vector
            def _(dve):
                dve.wait_ge(win_in, 80)
                split(dve, w_in_hi[:], w_in_lo[:], w_in[:], win_split, 0)
                dve.wait_ge(wo_in, 16)
                split(dve, wo_hi[:], wo_lo[:], wo[:], wo_split, 0)
                dve.wait_ge(ones_set, 1)

                def body(t, j, u, on):
                    if on(0):
                        need(dve, x_in[u], 16 * (j + 1))
                        need(dve, xT_ps, t - 1)
                        dve.tensor_copy(x_stack[:, u, :, 0:PATCH], x_tok[:, u]).then_inc(x_hi, 1)
                        dve.tensor_copy(x_stack[:, u, :, PATCH:2 * PATCH], x_tok[:, u]).then_inc(x_hi, 1)
                        need(dve, x_hi, 2 * t + 2)
                        dve.tensor_tensor(x_stack[:, u, :, 2 * PATCH:3 * PATCH], x_tok[:, u],
                                          x_stack[:, u, :, 0:PATCH].bitcast(F32), ALU.subtract).then_inc(x_lo, 1)
                    if on(1):
                        _, slot = at_lag(j, u, 1)
                        for k in range(KM):
                            n = KM * (t - 1) + k
                            need(dve, silu_done, n + 1)
                            if k == 0:
                                need(dve, out_ps, 2 * (t - 2))
                            dve.tensor_copy(hid_hi[:, slot, k], hid[:, k % 2]).then_inc(hi_done, 1)
                            need(dve, hi_done, n + 1)
                            dve.tensor_tensor(hid_lo[:, slot, k], hid[:, k % 2], hid_hi[:, slot, k].bitcast(F32),
                                              ALU.subtract).then_inc(lo_done, 1)

                run_steps(dve, GROUPS, 2, body)

            @block.tensor
            def _(pe):
                pe.wait_ge(stacked, 80)
                pe.wait_ge(wo_split, 2)

                def tokens(t, u):
                    need(pe, x_lo, t + 1)
                    need(pe, xT_ready, t)
                    for r in range(GROUP):
                        last = pe.transpose(ps_T[0:STACK, r * P:(r + 1) * P], x_stack[:, u, r].bitcast(F32),
                                            c["ident"][:])
                    last.then_inc(xT_ps, 1)

                def row_out(t, slot, r):
                    if r == 0:
                        need(pe, lo_done, KM * (t - 1))
                    if r % 2 == 0:
                        need(pe, out_sb, 2 * (t - 3) + r // 2 + 1)
                    out = ps_out[:, r // 2, (r % 2) * D:(r % 2 + 1) * D]
                    tok = slice(r * P, (r + 1) * P)
                    first = pe.matmul(out, xT[:, slot, tok], w_stack[:, MID:NW], start=True, stop=False)
                    if r == GROUP - 1:
                        first.then_inc(xT_used, 1)
                    for k in range(KM):
                        pe.matmul(out, hid_hi[:, slot, k, tok], wo_hi[:, k], start=False, stop=False)
                        pe.matmul(out, hid_hi[:, slot, k, tok], wo_lo[:, k], start=False, stop=False)
                        last = pe.matmul(out, hid_lo[:, slot, k, tok], wo_hi[:, k], start=False, stop=(k == KM - 1))
                    if r % 2:
                        last.then_inc(out_ps, 1)

                def body(t, j, u, on):
                    for k in range(KM):
                        if on(0) and k == KM - 1:
                            tokens(t, u)
                        if on(1):
                            n = KM * (t - 1) + k
                            if k == 0:
                                need(pe, xT_ready, t)
                            need(pe, silu_done, n - 3)
                            pe.matmul(ps_hid[:, k % 4], w_stack[:, k * P:(k + 1) * P], xT[:, (u - 1) % 2],
                                      start=True, stop=True).then_inc(hid_ps, 1)
                        if on(2) and k % 2:
                            row_out(t, at_lag(j, u, 2)[1], k // 2)

                run_steps(pe, GROUPS, 2, body)
        m.end()


def identity_attention(nc, c, h_in, h_out, n_out):
    W = 2 * IHD
    with ExitStack() as ctx:
        m = Memory(nc, ctx, "ident")
        h = m.sb("h", [P, 2, D])
        h_res = m.sb("h_res", [P, 2, D])
        stats = m.sb("stats", [P, 6])
        mv = m.sb("mv", [P, 2])
        var = m.sb("var", [P, 1])
        rstd = m.sb("rstd", [P, 1])
        v1 = m.sb("v1", [P, 4, IH, W])
        cent = m.sb("cent", [P, IH, W])
        cT = m.sb("cT", [P, 2, 4, P])
        cT_diag = m.sb("cT_diag", [P, 2, 4, 4, P])
        top = m.sb("top", [P, IH])
        left1 = m.sb("left1", [P, IH])
        left2 = m.sb("left2", [P, IH])
        parts = m.sb("parts", [P, P // IH, IH], BF16)
        partsT = m.sb("partsT", [3 * IH, P], BF16)
        E = m.sb("E", [P, 2, 4, 512])
        outT = m.sb("outT", [P, 2, 4, P])
        rsum = m.sb("rsum", [P, IH])
        att = m.sb("att", [P, IH, IHD])
        h2 = m.sb("h2", [P, 2, D])
        stats2 = m.sb("stats2", [P, 6])
        scratch = m.sb("scratch", [P, 1])
        mv2 = m.sb("mv2", [P, 2])
        var2 = m.sb("var2", [P, 1])
        rstd2 = m.sb("rstd2", [P, 1])
        n2 = m.sb("n2", [P, 2, D])
        banks = c["banks"]
        ps_S = banks[:, 0:4]
        ps_out = banks[:, 4].rearrange("p (h d) -> p h d", d=W)
        ps_mean = banks[:, 5, 0:D].rearrange("p (h d) -> p h d", d=IHD)
        ps_cT = banks[:, 6].rearrange("p (j n) -> p j n", n=P)
        ps_mT = banks[:, 7, 0:P // 2].bitcast(BF16)

        h_ld, res_ld = [m.sem("h_ld0"), m.sem("h_ld1")], [m.sem("res_ld0"), m.sem("res_ld1")]
        stored = [m.sem("st0"), m.sem("st1")]
        pads = m.sem("pads")
        s = {n: m.sem(n) for n in (
            "stat", "rstd_done", "norm", "mean_ps", "centred", "cT_ps", "cT_ready", "S_ps", "max_done", "split_done",
            "mT_ps", "mT_ready", "shifted", "exp_done", "outT_ps",
            "outT_ready", "out_ps", "recip", "scaled", "h2_done", "stat2", "rstd2_done",
            "n2_done")}
        heads = [(j, k, 4 * j + k) for j in range(4) for k in range(4)]

        with nc.Block() as block:

            @block.sync
            def _(sp):
                def body(t, j, u, on):
                    if on(0):
                        need(sp, s["norm"], t - 1)
                        sp.dma_start(h[:, u % 2], h_in[t]).then_inc(h_ld[u % 2], 16)
                    if on(4):
                        slot = u % 2
                        need(sp, s["h2_done"], t - 5)
                        sp.dma_start(h_res[:, slot], h_in[t - 4]).then_inc(res_ld[slot], 16)
                    if on(5):
                        slot = (u - 5) % 2
                        need(sp, s["n2_done"], t - 4)
                        sp.dma_start(h_out[t - 5], h2[:, slot]).then_inc(stored[slot], 16)
                        sp.dma_start(n_out[t - 5], n2[:, slot]).then_inc(stored[slot], 16)

                run_steps(sp, ROWS, 5, body, unroll=4)
                for st in stored:
                    sp.wait_ge(st, 32 * ROWS // 2)

            @block.gpsimd
            def _(pool):
                pool.memset(v1[:], 1.0).then_inc(pads, 1)
                pool.memset(cent[:], 0.0).then_inc(pads, 1)
                pool.memset(cT_diag[:], 0.0).then_inc(pads, 1)
                pool.memset(parts[:], 0.0).then_inc(pads, 1)

                def body(t, j, u, on):
                    if on(0):
                        need(pool, s["stat"], 3 * (t + 1))
                        need(pool, s["norm"], t)
                        pool.tensor_tensor(rstd[:], var[:], c["neg_half"][:, 0:1], ALU.pow).then_inc(s["rstd_done"], 1)
                    if on(4):
                        need(pool, s["stat2"], 3 * (t - 3))
                        need(pool, s["n2_done"], t - 4)
                        pool.tensor_tensor(rstd2[:], var2[:], c["neg_half"][:, 0:1], ALU.pow).then_inc(s["rstd2_done"], 1)

                run_steps(pool, ROWS, 4, body, unroll=4)

            @block.scalar
            def _(act):
                act.wait_ge(pads, 4)

                def body(t, j, u, on):
                    if on(1):
                        need(act, s["cT_ps"], t)
                        need(act, s["S_ps"], 4 * (t - 2))
                        act.activation(cT[:, (u - 1) % 2], ps_cT, ACT.Copy).then_inc(s["cT_ready"], 1)
                        for k in range(4):
                            own = slice(W * k, W * k + W)
                            act.activation(cT_diag[own, (u - 1) % 2, :, k], ps_cT[own], ACT.Copy
                                           ).then_inc(s["cT_ready"], 1)
                    if on(3):
                        need(act, s["outT_ps"], t - 2)
                        need(act, s["out_ps"], t - 4)
                        act.activation(outT[:, (u - 3) % 2], ps_cT, ACT.Copy).then_inc(s["outT_ready"], 1)
                    if on(2):
                        b = t - 2
                        need(act, s["mT_ps"], b + 1)
                        need(act, s["shifted"], 4 * b)
                        act.activation(partsT[:], ps_mT[0:3 * IH], ACT.Copy).then_inc(s["mT_ready"], 1)
                        for k in range(4):
                            need(act, s["shifted"], 4 * b + k + 1)
                            need(act, s["outT_ps"], b - 1)
                            act.activation(E[:, u % 2, k], ps_S[:, k], ACT.Exp).then_inc(s["exp_done"], 1)

                run_steps(act, ROWS, 4, body, unroll=4)

            @block.vector
            def _(dve):
                dve.wait_ge(pads, 4)

                def body(t, j, u, on):
                    if on(0):
                        half, slot = at_lag(j, u, 0)
                        need(dve, h_ld[slot], 16 * (half + 1))
                        dve.bn_stats(stats[:], h[:, slot]).then_inc(s["stat"], 1)
                        need(dve, s["stat"], 3 * t + 1)
                        take_wait(dve, scratch[:])
                        dve.bn_aggr(mv[:], stats[:]).then_inc(s["stat"], 1)
                        need(dve, s["stat"], 3 * t + 2)
                        need(dve, s["rstd_done"], t)
                        dve.tensor_scalar(var[:], mv[:, 1:2], EPS, None, ALU.add).then_inc(s["stat"], 1)
                    if on(0):
                        need(dve, s["rstd_done"], t + 1)
                        need(dve, s["outT_ps"], t - 3)
                        dve.tensor_scalar(v1[:, u, :, 0:IHD], h[:, u % 2].rearrange("p (h d) -> p h d", d=IHD),
                                          mv[:, 0:1], rstd[:], ALU.subtract, ALU.mult).then_inc(s["norm"], 1)
                    if on(2):
                        b = t - 2
                        for k in range(4):
                            need(dve, s["S_ps"], 4 * b + k + 1)
                            if k == 0:
                                need(dve, s["split_done"], 5 * b)
                            dve.tensor_reduce(top[:, 4 * k:4 * k + 4],
                                              ps_S[:, k].rearrange("p (j t) -> p j t", j=4), AX_X, ALU.max
                                              ).then_inc(s["max_done"], 1)
                        n = 5 * b
                        need(dve, s["max_done"], 4 * b + 4)
                        need(dve, s["mT_ps"], b)
                        dve.tensor_copy(parts[:, 0], top[:]).then_inc(s["split_done"], 1)
                        need(dve, s["split_done"], n + 1)
                        dve.tensor_tensor(left1[:], top[:], parts[:, 0], ALU.subtract).then_inc(s["split_done"], 1)
                        need(dve, s["split_done"], n + 2)
                        dve.tensor_copy(parts[:, 1], left1[:]).then_inc(s["split_done"], 1)
                        need(dve, s["split_done"], n + 3)
                        dve.tensor_tensor(left2[:], left1[:], parts[:, 1], ALU.subtract).then_inc(s["split_done"], 1)
                        need(dve, s["split_done"], n + 4)
                        dve.tensor_copy(parts[:, 2], left2[:]).then_inc(s["split_done"], 1)
                    if on(4):
                        b = t - 4
                        half, slot = at_lag(j, u, 4)
                        need(dve, s["out_ps"], b + 1)
                        need(dve, s["scaled"], b)
                        dve.reciprocal(rsum[:], ps_out[:, :, IHD]).then_inc(s["recip"], 1)
                        need(dve, s["recip"], b + 1)
                        need(dve, s["h2_done"], b)
                        dve.tensor_tensor(att[:], ps_out[:, :, 0:IHD], rsum[:].unsqueeze(2).to_broadcast([P, IH, IHD]),
                                          ALU.mult).then_inc(s["scaled"], 1)
                        need(dve, s["scaled"], b + 1)
                        need(dve, res_ld[slot], 16 * (half + 1))
                        need(dve, stored[slot], 32 * half)
                        dve.tensor_tensor(h2[:, slot], att[:].rearrange("p h d -> p (h d)"), h_res[:, slot],
                                          ALU.add).then_inc(s["h2_done"], 1)
                    if on(0):
                        need(dve, s["norm"], t + 1)
                        need(dve, s["mean_ps"], t + 1)
                        need(dve, s["cT_ps"], t)
                        dve.tensor_tensor(cent[:, :, 0:IHD], v1[:, u, :, 0:IHD], ps_mean, ALU.subtract
                                          ).then_inc(s["centred"], 1)
                    if on(4):
                        need(dve, s["h2_done"], b + 1)
                        dve.bn_stats(stats2[:], h2[:, slot]).then_inc(s["stat2"], 1)
                        need(dve, s["stat2"], 3 * b + 1)
                        take_wait(dve, scratch[:])
                        dve.bn_aggr(mv2[:], stats2[:]).then_inc(s["stat2"], 1)
                        need(dve, s["stat2"], 3 * b + 2)
                        need(dve, s["rstd2_done"], b)
                        dve.tensor_scalar(var2[:], mv2[:, 1:2], EPS, None, ALU.add).then_inc(s["stat2"], 1)
                        need(dve, s["rstd2_done"], b + 1)
                        dve.tensor_scalar(n2[:, slot], h2[:, slot], mv2[:, 0:1], rstd2[:], ALU.subtract, ALU.mult
                                          ).then_inc(s["n2_done"], 1)

                run_steps(dve, ROWS, 4, body, unroll=4)

            @block.tensor
            def _(pe):
                def body(t, j, u, on):
                    if on(1):
                        need(pe, s["centred"], t)
                        need(pe, s["cT_ready"], 5 * (t - 1))
                        need(pe, s["outT_ready"], t - 3)
                        for i in range(4):
                            last = pe.transpose(ps_cT[:, i], cent[:, 4 * i:4 * i + 4].rearrange("p h d -> p (h d)"),
                                                c["ident"][:])
                        last.then_inc(s["cT_ps"], 1)
                    if on(2):
                        b, slot = t - 2, u % 2
                        need(pe, s["cT_ready"], 5 * (b + 1))
                        for j in range(4):
                            need(pe, s["exp_done"], 4 * (b - 1) + j + 1)
                            pe.matmul(ps_S[:, j], cT[:, slot, j], cT_diag[:, slot, j].rearrange("p k n -> p (k n)"),
                                      start=True, stop=False, skip_group_check=True).then_inc(s["S_ps"], 1)
                    if on(3):
                        b = t - 3
                        need(pe, s["exp_done"], 4 * b + 4)
                        need(pe, s["cT_ready"], 5 * (t if on(1) else ROWS))
                        for j, k, head in heads:
                            last = pe.matmul(ps_cT[W * k:W * k + W, j], v1[:, (u - 3) % 4, head],
                                             E[:, (u - 3) % 2, j, k * P:(k + 1) * P], start=True, stop=True,
                                             skip_group_check=True)
                        last.then_inc(s["outT_ps"], 1)
                    if on(0):
                        need(pe, s["norm"], t + 1)
                        need(pe, s["centred"], t)
                        pe.matmul(ps_mean, c["mean"][:], v1[:, u, :, 0:IHD], start=True, stop=True
                                  ).then_inc(s["mean_ps"], 1)
                    if on(4):
                        need(pe, s["outT_ready"], t - 3)
                        need(pe, s["scaled"], t - 4)
                        for i in range(4):
                            last = pe.transpose(ps_out[:, 4 * i:4 * i + 4].rearrange("p h d -> p (h d)"),
                                                outT[:, u % 2, i], c["ident"][:])
                        last.then_inc(s["out_ps"], 1)
                    if on(2):
                        b = t - 2
                        need(pe, s["split_done"], 5 * b + 5)
                        need(pe, s["mT_ready"], b)
                        pe.transpose(ps_mT, parts[:].rearrange("p a h -> p (a h)"), c["ident_b"][:]
                                     ).then_inc(s["mT_ps"], 1)
                    if on(2):
                        b = t - 2
                        need(pe, s["mT_ready"], b + 1)
                        for j, k, head in heads:
                            last = pe.matmul(ps_S[:, j, k * P:(k + 1) * P], c["sel"][:, head], partsT[:],
                                             start=False, stop=(k == 3), skip_group_check=True)
                            if k == 3:
                                last.then_inc(s["shifted"], 1)

                run_steps(pe, ROWS, 4, body, unroll=4)
        m.end()


def layer_attention(nc, c, layer, wqkv, q_scale, k_scale, wo, cos, sin, x_in, x_out):
    NQ = 3 * INNER // 512
    half = HD // 2
    with ExitStack() as ctx:
        m = Memory(nc, ctx, f"attn{layer}")
        w = m.sb("w", [P, KD, 3 * INNER])
        w_hi = m.sb("w_hi", [P, KD, 3 * INNER], F32R)
        w_lo = m.sb("w_lo", [P, KD, 3 * INNER], F32R)
        wo_f = m.sb("wo_f", [P, KI, D])
        wo_hi = m.sb("wo_hi", [P, KI, D], F32R)
        wo_lo = m.sb("wo_lo", [P, KI, D], F32R)
        scales = m.sb("scales", [P, 2, HD])
        cos_t = m.sb("cos_t", [P, 2, HD])
        sin_t = m.sb("sin_t", [P, 2, HD])
        cos_s = m.sb("cos_s", [P, 2, 1, HD])
        sin_s = m.sb("sin_s", [P, 2, 1, HD])
        x = m.sb("x_", [P, 2, D])
        x_res = m.sb("x_res", [P, 2, D])
        xT_hi = m.sb("xT_hi", [P, 2, KD, P], F32R)
        xT_lo = m.sb("xT_lo", [P, 2, KD, P], F32R)
        sq = m.sb("sq", [P, 2 * HEADS, HD])
        ss = m.sb("ss", [P, 2 * HEADS])
        ssm = m.sb("ssm", [P, 2 * HEADS])
        rn = m.sb("rn", [P, 2, 2 * HEADS])
        rot_a = m.sb("rot_a", [P, 2, HEADS, HD])
        rot_b = m.sb("rot_b", [P, 2, HEADS, HD])
        qk = m.sb("qk", [P, 2, 2, HEADS * HD])
        v = m.sb("v", [P, 2, INNER])
        qT = m.sb("qT", [P, KI, P])
        kT = m.sb("kT", [P, KI, P])
        neg_top = m.sb("neg_top", [P, 2, HEADS // 2])
        nbias = m.sb("nbias", [P, 2, HEADS // 2])
        E = m.sb("E", [P, 2, HEADS // 2, P])
        sums = m.sb("sums", [P, 2, 2, HEADS // 2])
        ET = m.sb("ET", [P, 2, HEADS // 2, P])
        rsum = m.sb("rsum", [P, 2, HEADS // 2])
        o = m.sb("o", [P, INNER])
        oT_hi = m.sb("oT_hi", [P, KI, P], F32R)
        oT_lo = m.sb("oT_lo", [P, KI, P], F32R)
        x_new = m.sb("x_new", [P, 2, D])
        banks = c["banks"]
        ps_qkv = banks[:, 0:3]
        ps_q = banks[:, 3]
        ps_k = banks[:, 4]
        ps_s = banks[:, 5:7]
        ps_x = banks[:, 7]

        x_ld, res_ld = [m.sem("x_ld0"), m.sem("x_ld1")], [m.sem("res_ld0"), m.sem("res_ld1")]
        stored = [m.sem("st0"), m.sem("st1")]
        w_ld, wo_ld, tab_ld, w_split, wo_split, tabs, pads = [
            m.sem(n) for n in ("w_ld", "wo_ld", "tab_ld", "w_split", "wo_split", "tabs", "pads")]
        s = {n: m.sem(n) for n in (
            "xT_ps", "xT_hi", "xT_lo", "qkv_ps", "squared", "normed", "rn_done", "rot_a", "rot_b", "roped", "qk_done",
            "v_done", "q_ps", "k_ps", "qT_done", "kT_done", "s_ps", "top_done", "nbias_done", "exp_done", "e_ps",
            "et_act", "et_dve", "o_ps", "rsum_done", "o_done", "oT_ps", "oT_hi", "oT_lo", "out_ps", "x_done")}

        with nc.Block() as block:

            @block.sync
            def _(sp):
                for k in range(KD):
                    sp.dma_start(w[:, k], wqkv[layer, k * P:(k + 1) * P]).then_inc(w_ld, 16)
                sp.dma_start(wo_f[:], wo[layer].rearrange("(k p) n -> p k n", p=P)).then_inc(wo_ld, 16)
                for n, src in enumerate((q_scale, k_scale)):
                    sp.dma_start(scales[:, n], src[layer].partition_broadcast(P)).then_inc(tab_ld, 16)
                sp.dma_start(cos_t[:], cos).then_inc(tab_ld, 16)
                sp.dma_start(sin_t[:], sin).then_inc(tab_ld, 16)

                def body(t, j, u, on):
                    if on(0):
                        need(sp, s["xT_ps"], t - 1)
                        sp.dma_start(x[:, u], x_in[t]).then_inc(x_ld[u], 16)
                    if on(4):
                        slot = (u - 4) % 2
                        need(sp, s["x_done"], t - 5)
                        sp.dma_start(x_res[:, slot], x_in[t - 4]).then_inc(res_ld[slot], 16)
                    if on(5):
                        slot = (u - 5) % 2
                        need(sp, s["x_done"], t - 4)
                        sp.dma_start(x_out[t - 5], x_new[:, slot]).then_inc(stored[slot], 16)

                run_steps(sp, ROWS, 5, body)
                for st in stored:
                    sp.wait_ge(st, 16 * ROWS // 2)

            @block.gpsimd
            def _(pool):
                pool.memset(xT_hi[:, :, 1, 0:1].bitcast(F32), 0.0).then_inc(pads, 1)
                pool.memset(xT_lo[:, :, 1, 0:1].bitcast(F32), 0.0).then_inc(pads, 1)

                def body(t, j, u, on):
                    if on(1):
                        b, slot = t - 1, (u - 1) % 2
                        need(pool, s["normed"], 2 * b + 2)
                        need(pool, s["exp_done"], b - 1)
                        pool.tensor_tensor(rn[:, slot], ssm[:], c["neg_half"][:], ALU.pow).then_inc(s["rn_done"], 1)
                        need(pool, s["rot_a"], b + 1)
                        need(pool, s["rot_b"], 2 * b + 2)
                        need(pool, s["k_ps"], b - 1)
                        pool.tensor_tensor(qk[:, slot].rearrange("p a n -> p (a n)"),
                                           rot_a[:].rearrange("p a h d -> p (a h d)"),
                                           rot_b[:].rearrange("p a h d -> p (a h d)"), ALU.add).then_inc(s["roped"], 1)
                        need(pool, s["rn_done"], b + 1)
                        need(pool, s["roped"], b + 1)
                        kh = qk[:, slot, 1].rearrange("p (h d) -> p h d", d=HD)
                        pool.tensor_tensor(kh, kh, rn[:, slot, HEADS:].unsqueeze(2).to_broadcast([P, HEADS, HD]),
                                           ALU.mult).then_inc(s["qk_done"], 1)

                run_steps(pool, ROWS, 4, body)

            @block.scalar
            def _(act):
                act.wait_ge(pads, 2)

                def body(t, j, u, on):
                    if on(1):
                        b = t - 1
                        need(act, s["qkv_ps"], 3 * b + 2)
                        need(act, s["normed"], 2 * b - 1)
                        act.activation(sq[:].rearrange("p h d -> p (h d)"), ps_qkv[:, 0:2].rearrange("p a n -> p (a n)"),
                                       ACT.Square).then_inc(s["squared"], 1)
                    if on(2):
                        b = t - 2
                        need(act, s["q_ps"], b + 1)
                        need(act, s["s_ps"], b)
                        act.activation(qT[:].rearrange("p k n -> p (k n)"), ps_q[:], ACT.Copy).then_inc(s["qT_done"], 1)
                    if on(3):
                        b = t - 3
                        need(act, s["e_ps"], 2 * b + 1)
                        need(act, s["o_ps"], b)
                        act.activation(ET[:, 0].rearrange("p i n -> p (i n)"), ps_s[:, 0], ACT.Copy).then_inc(s["et_act"], 1)
                    if on(4):
                        b = t - 4
                        need(act, s["oT_ps"], b + 1)
                        need(act, s["out_ps"], b)
                        act.activation(oT_hi[:].rearrange("p k n -> p (k n)"), ps_x[:], ACT.Copy).then_inc(s["oT_hi"], 1)
                    if on(0):
                        need(act, s["xT_ps"], t + 1)
                        need(act, s["qkv_ps"], 3 * (t - 1))
                        act.activation(xT_hi[:, u, 0], ps_x[:, 0:P], ACT.Copy).then_inc(s["xT_hi"], 1)
                        act.activation(xT_hi[:, u, 1, 1:P], ps_x[:, P:2 * P - 1], ACT.Copy).then_inc(s["xT_hi"], 1)
                    if on(2):
                        b, slot = t - 2, u
                        need(act, s["nbias_done"], b + 1)
                        need(act, s["e_ps"], 2 * b)
                        need(act, s["rsum_done"], b - 1)
                        for r in range(2):
                            for i in range(HEADS // 2):
                                last = act.activation(E[:, r, i], ps_s[:, r, i * P:(i + 1) * P], ACT.Exp,
                                                      bias=nbias[:, r, i:i + 1], scale=rn[:, slot, 2 * i + r:2 * i + r + 1],
                                                      accum_out=sums[:, slot, r, i:i + 1])
                        last.then_inc(s["exp_done"], 1)
                    if on(1):
                        b, slot = t - 1, (u - 1) % 2
                        need(act, s["qkv_ps"], 3 * b + 3)
                        need(act, s["o_ps"], b - 1)
                        act.activation(v[:, slot], ps_qkv[:, 2], ACT.Copy).then_inc(s["v_done"], 1)

                run_steps(act, ROWS, 4, body)

            @block.vector
            def _(dve):
                for k in range(KD):
                    dve.wait_ge(w_ld, 16 * KD)
                    split(dve, w_hi[:, k], w_lo[:, k], w[:, k], w_split, 2 * k)
                dve.wait_ge(wo_ld, 16)
                split(dve, wo_hi[:], wo_lo[:], wo_f[:], wo_split, 0)
                dve.wait_ge(tab_ld, 64)
                dve.tensor_tensor(cos_s[:, :, 0], cos_t[:], scales[:], ALU.mult).then_inc(tabs, 1)
                dve.tensor_tensor(sin_s[:, :, 0, 0:half], sin_t[:, :, 0:half], scales[:, :, half:HD], ALU.mult
                                  ).then_inc(tabs, 1)
                dve.tensor_tensor(sin_s[:, :, 0, half:HD], sin_t[:, :, half:HD], scales[:, :, 0:half], ALU.mult
                                  ).then_inc(tabs, 1)
                dve.wait_ge(tabs, 3)
                dve.wait_ge(pads, 2)
                qk_ps = ps_qkv[:, 0:2].rearrange("p a (h d) -> p a h d", d=HD)

                def body(t, j, u, on):
                    if on(1):
                        b = t - 1
                        need(dve, s["squared"], b + 1)
                        need(dve, s["rn_done"], b)
                        dve.tensor_reduce(ss[:], sq[:], AX_X, ALU.add).then_inc(s["normed"], 1)
                        need(dve, s["normed"], 2 * b + 1)
                        dve.tensor_scalar(ssm[:], ss[:], 1e-24, None, ALU.max).then_inc(s["normed"], 1)
                    if on(2):
                        b = t - 2
                        need(dve, s["k_ps"], b + 1)
                        need(dve, s["s_ps"], b)
                        dve.tensor_copy(kT[:].rearrange("p k n -> p (k n)"), ps_k[:]).then_inc(s["kT_done"], 1)
                    if on(3):
                        b = t - 3
                        need(dve, s["e_ps"], 2 * b + 2)
                        need(dve, s["o_ps"], b)
                        dve.tensor_copy(ET[:, 1].rearrange("p i n -> p (i n)"), ps_s[:, 1]).then_inc(s["et_dve"], 1)
                    if on(4):
                        b = t - 4
                        need(dve, s["oT_hi"], b + 1)
                        need(dve, s["out_ps"], b)
                        dve.tensor_tensor(oT_lo[:].rearrange("p k n -> p (k n)"), ps_x[:],
                                          oT_hi[:].rearrange("p k n -> p (k n)").bitcast(F32), ALU.subtract
                                          ).then_inc(s["oT_lo"], 1)
                    if on(1):
                        b = t - 1
                        need(dve, s["squared"], b + 1)
                        need(dve, s["roped"], b)
                        for a in range(2):
                            last = dve.tensor_tensor(rot_a[:, a], qk_ps[:, a],
                                                     cos_s[:, a].to_broadcast([P, HEADS, HD]), ALU.mult)
                        last.then_inc(s["rot_a"], 1)
                    if on(2):
                        b, slot = t - 2, u
                        need(dve, s["s_ps"], b + 1)
                        need(dve, s["nbias_done"], b)
                        dve.tensor_reduce(neg_top[:], ps_s[:].rearrange("p r (i n) -> p r i n", n=P), AX_X, ALU.max,
                                          negate=True).then_inc(s["top_done"], 1)
                        need(dve, s["top_done"], b + 1)
                        need(dve, s["rn_done"], b + 1)
                        need(dve, s["exp_done"], b)
                        dve.tensor_tensor(nbias[:], neg_top[:], rn[:, slot, 0:HEADS].rearrange("p (i r) -> p r i", r=2),
                                          ALU.mult).then_inc(s["nbias_done"], 1)
                    if on(0):
                        need(dve, s["xT_hi"], 2 * t + 2)
                        dve.tensor_tensor(xT_lo[:, u, 0], ps_x[:, 0:P], xT_hi[:, u, 0].bitcast(F32), ALU.subtract
                                          ).then_inc(s["xT_lo"], 1)
                        dve.tensor_tensor(xT_lo[:, u, 1, 1:P], ps_x[:, P:2 * P - 1], xT_hi[:, u, 1, 1:P].bitcast(F32),
                                          ALU.subtract).then_inc(s["xT_lo"], 1)
                    if on(1):
                        b = t - 1
                        for a in range(2):
                            for lo_, hi_ in ((0, half), (half, 0)):
                                last = dve.tensor_tensor(rot_b[:, a, :, lo_:lo_ + half], qk_ps[:, a, :, hi_:hi_ + half],
                                                         sin_s[:, a, :, lo_:lo_ + half].to_broadcast([P, HEADS, half]),
                                                         ALU.mult)
                            last.then_inc(s["rot_b"], 1)
                    if on(3):
                        b, slot = t - 3, (u - 3) % 2
                        need(dve, s["exp_done"], b + 1)
                        dve.reciprocal(rsum[:], sums[:, slot]).then_inc(s["rsum_done"], 1)
                        need(dve, s["rsum_done"], b + 1)
                        need(dve, s["o_ps"], b + 1)
                        need(dve, s["oT_ps"], b)
                        dve.tensor_tensor(o[:].rearrange("p (i r d) -> p i r d", r=2, d=HD),
                                          ps_q[:].rearrange("p (i r d) -> p i r d", r=2, d=HD),
                                          rsum[:].rearrange("p r i -> p i r").unsqueeze(3).to_broadcast(
                                              [P, HEADS // 2, 2, HD]), ALU.mult).then_inc(s["o_done"], 1)
                    if on(4):
                        b = t - 4
                        hf, slot = at_lag(j, u, 4)
                        need(dve, s["out_ps"], b + 1)
                        need(dve, res_ld[slot], 16 * (hf + 1))
                        need(dve, stored[slot], 16 * hf)
                        dve.tensor_tensor(x_new[:, slot], ps_k[:, 0:D], x_res[:, slot], ALU.add).then_inc(s["x_done"], 1)

                run_steps(dve, ROWS, 4, body)

            @block.tensor
            def _(pe):
                pe.wait_ge(w_split, 2 * KD)
                pe.wait_ge(wo_split, 2)

                def body(t, j, u, on):
                    if on(1):
                        b, slot = t - 1, (u - 1) % 2
                        need(pe, s["xT_hi"], 2 * b + 2)
                        need(pe, s["xT_lo"], 2 * b + 2)
                        for n in range(NQ):
                            if n == 0:
                                need(pe, s["squared"], b)
                                need(pe, s["rot_a"], b)
                                need(pe, s["rot_b"], 2 * b)
                            if n == 2:
                                need(pe, s["v_done"], b)
                            cols = slice(n * 512, (n + 1) * 512)
                            for k in range(KD):
                                pe.matmul(ps_qkv[:, n], xT_hi[:, slot, k], w_hi[:, k, cols], start=(k == 0), stop=False)
                                pe.matmul(ps_qkv[:, n], xT_hi[:, slot, k], w_lo[:, k, cols], start=False, stop=False)
                                last = pe.matmul(ps_qkv[:, n], xT_lo[:, slot, k], w_hi[:, k, cols], start=False,
                                                 stop=(k == KD - 1))
                            last.then_inc(s["qkv_ps"], 1)
                    if on(2):
                        b, slot = t - 2, u
                        need(pe, s["qk_done"], b + 1)
                        for a, dst, free, done in ((0, ps_q, "o_done", "q_ps"), (1, ps_k, "x_done", "k_ps")):
                            need(pe, s[free], b - 1 if a == 0 else b - 2)
                            for k in range(KI):
                                last = pe.transpose(dst[:, k * P:(k + 1) * P], qk[:, slot, a, k * P:(k + 1) * P],
                                                    c["ident"][:])
                            last.then_inc(s[done], 1)
                    if on(3):
                        b = t - 3
                        need(pe, s["exp_done"], b + 1)
                        for r in range(2):
                            for i in range(HEADS // 2):
                                last = pe.transpose(ps_s[:, r, i * P:(i + 1) * P], E[:, r, i], c["ident"][:])
                            last.then_inc(s["e_ps"], 1)
                    if on(4):
                        b = t - 4
                        need(pe, s["o_done"], b + 1)
                        need(pe, s["xT_lo"], 2 * min_int(t, ROWS))
                        for k in range(KI):
                            last = pe.transpose(ps_x[:, k * P:(k + 1) * P], o[:, k * P:(k + 1) * P], c["ident"][:])
                        last.then_inc(s["oT_ps"], 1)
                    if on(2):
                        b = t - 2
                        need(pe, s["qT_done"], b + 1)
                        need(pe, s["kT_done"], b + 1)
                        need(pe, s["et_act"], b)
                        need(pe, s["et_dve"], b)
                        for r in range(2):
                            pe.matmul(ps_s[:, r], c["ident_b"][:], c["causal"][:].rearrange("p i n -> p (i n)"),
                                      start=True, stop=False, skip_group_check=True)
                            part = slice(r * HD, (r + 1) * HD)
                            for i in range(HEADS // 2):
                                last = pe.matmul(ps_s[:, r, i * P:(i + 1) * P], qT[part, i], kT[part, i], start=False,
                                                 stop=True, skip_group_check=True)
                        last.then_inc(s["s_ps"], 1)
                    if on(0):
                        need(pe, x_ld[u], 16 * (j + 1))
                        need(pe, s["xT_lo"], 2 * t)
                        need(pe, s["oT_lo"], t - 3)
                        for k in range(KD):
                            last = pe.transpose(ps_x[:, k * P:(k + 1) * P], x[:, u, k * P:(k + 1) * P], c["ident"][:])
                        last.then_inc(s["xT_ps"], 1)
                    if on(3):
                        b, slot = t - 3, (u - 3) % 2
                        need(pe, s["et_act"], b + 1)
                        need(pe, s["et_dve"], b + 1)
                        need(pe, s["v_done"], b + 1)
                        need(pe, s["qT_done"], min_int(t - 1, ROWS))
                        for i in range(HEADS // 2):
                            for r in range(2):
                                h = 2 * i + r
                                last = pe.matmul(ps_q[:, h * HD:(h + 1) * HD], ET[:, r, i], v[:, slot, h * HD:(h + 1) * HD],
                                                 start=True, stop=True)
                        last.then_inc(s["o_ps"], 1)
                    if on(4):
                        b = t - 4
                        need(pe, s["oT_hi"], b + 1)
                        need(pe, s["oT_lo"], b + 1)
                        need(pe, s["kT_done"], min_int(t - 1, ROWS))
                        need(pe, s["x_done"], b)
                        for k in range(KI):
                            pe.matmul(ps_k[:, 0:D], oT_hi[:, k], wo_hi[:, k], start=(k == 0), stop=False)
                            pe.matmul(ps_k[:, 0:D], oT_hi[:, k], wo_lo[:, k], start=False, stop=False)
                            last = pe.matmul(ps_k[:, 0:D], oT_lo[:, k], wo_hi[:, k], start=False, stop=(k == KI - 1))
                        last.then_inc(s["out_ps"], 1)

                run_steps(pe, ROWS, 4, body)
        m.end()


def layer_forward(nc, c, layer, ln_g, ln_b, w1, b1, w2, b2, x_in, x_out, extra=None):
    with ExitStack() as ctx:
        m = Memory(nc, ctx, f"ffn{layer}")
        w1_f = m.sb("w1_f", [P, KD, 2, HPAD])
        w1_hi = m.sb("w1_hi", [P, KD, 2, HPAD], F32R)
        w1_lo = m.sb("w1_lo", [P, KD, 2, HPAD], F32R)
        w2_f = m.sb("w2_f", [P, KH, D])
        w2_hi = m.sb("w2_hi", [P, KH, D], F32R)
        w2_lo = m.sb("w2_lo", [P, KH, D], F32R)
        g_col = m.sb("g_col", [P, KD])
        b_col = m.sb("b_col", [P, KD])
        b1_in = m.sb("b1_in", [P, 2, KH])
        b1_col = m.sb("b1_col", [P, 2, KH])
        x = m.sb("x_", [P, 2, GROUP, D])
        x_res = m.sb("x_res", [P, GROUP, D])
        add = m.sb("add", [P, GROUP, D]) if extra is not None else None
        stats = m.sb("stats", [P, GROUP, 2, 6])
        scratch = m.sb("scratch", [P, 1])
        mv = m.sb("mv", [P, GROUP, 2])
        var = m.sb("var", [P, GROUP])
        rstd = m.sb("rstd", [P, GROUP])
        xn = m.sb("xn", [P, GROUP, D])
        xT_hi = m.sb("xT_hi", [P, 2, KD, GT], F32R)
        xT_lo = m.sb("xT_lo", [P, 2, KD, GT], F32R)
        gate = m.sb("gate", [P, 2, GT])
        gated = m.sb("gated", [P, 2, GT])
        h_hi = m.sb("h_hi", [P, 2, KH, GT], F32R)
        h_lo = m.sb("h_lo", [P, 2, KH, GT], F32R)
        x_new = m.sb("x_new", [P, GROUP, D])
        banks = c["banks"]
        ps_out = banks[:, 0, 0:D]
        ps_shift = banks[:, 1].rearrange("p (r n) -> p r n", n=P)
        ps_T = banks[:, 2:4]
        ps_h = banks[:, 4:8].rearrange("p (b a) n -> p b a n", a=2)

        x_ld = [m.sem("x_ld0"), m.sem("x_ld1")]
        w_ld, w2_ld, c_ld, w2_clear, w1_clear = [m.sem(n) for n in ("w_ld", "w2_ld", "c_ld", "w2_clear", "w1_clear")]
        w1_scaled, w1_split, w2_split, b1_ps, b1_done = [
            m.sem(n) for n in ("w1_scaled", "w1_split", "w2_split", "b1_ps", "b1_done")]
        h_pads, res_ld, stored = m.sem("h_pads"), m.sem("res_ld"), m.sem("stored")
        s = {n: m.sem(n) for n in (
            "shift_ps", "stat", "aggr", "eps_done", "rstd_done", "norm", "xT_ps", "xT_hi", "xT_lo", "h_ps", "gate_done",
            "gated_done", "h_hi", "h_lo", "out_ps", "x_done", "sum_done")}
        XT_AT = 3
        per_res = 32 if extra is not None else 16
        if extra is None:
            s["sum_done"] = s["x_done"]

        slow = {"allow_slow_non_contiguous": True}

        def rows(ap, t):
            return ap[bass.ds(GROUP * t, GROUP)].rearrange("b n f -> n b f")

        with nc.Block() as block:

            @block.sync
            def _(sp):
                sp.wait_ge(w1_clear, 2)
                for k in range(KD):
                    sp.dma_start(w1_f[:, k, :, 0:HID], w1[layer, k * P:(k + 1) * P].rearrange("p (a n) -> p a n", a=2)
                                 ).then_inc(w_ld, 16)
                sp.dma_start(g_col[:], ln_g[layer].rearrange("(k p) -> p k", p=P), **slow).then_inc(c_ld, 16)
                sp.dma_start(b_col[:], ln_b[layer].rearrange("(k p) -> p k", p=P), **slow).then_inc(c_ld, 16)
                full = (KH - 1) * P
                for a in range(2):
                    sp.dma_start(b1_in[:, a, 0:KH - 1], b1[layer, a * HID:a * HID + full].rearrange("(k p) -> p k", p=P),
                                 **slow).then_inc(c_ld, 16)
                    sp.dma_start(b1_in[0:HTAIL, a, KH - 1:KH],
                                 b1[layer, a * HID + full:(a + 1) * HID].rearrange("(p k) -> p k", k=1)).then_inc(c_ld, 16)
                sp.wait_ge(w2_clear, 1)
                sp.dma_start(w2_f[:, 0:KH - 1], w2[layer, 0:full].rearrange("(k p) n -> p k n", p=P)).then_inc(w2_ld, 16)
                sp.dma_start(w2_f[0:HTAIL, KH - 1], w2[layer, full:HID]).then_inc(w2_ld, 16)
                sp.dma_start(w2_f[BIAS_ROW:BIAS_ROW + 1, KH - 1], b2[layer].rearrange("(a n) -> a n", a=1)
                             ).then_inc(w2_ld, 16)

                def body(t, j, u, on):
                    if on(0):
                        need(sp, s["norm"], 2 * GROUP * (t - 1))
                        sp.dma_start(x[:, u], rows(x_in, t)).then_inc(x_ld[u], 16)
                    if on(3):
                        need(sp, s["sum_done"], GROUP * (t - 3))
                        sp.dma_start(x_res[:], rows(x_in, t - 3)).then_inc(res_ld, 16)
                        if extra is not None:
                            sp.dma_start(add[:], rows(extra, t - 3)).then_inc(res_ld, 16)
                        need(sp, s["sum_done"], GROUP * (t - 2))
                        sp.dma_start(rows(x_out, t - 3), x_new[:]).then_inc(stored, 16)

                run_steps(sp, GROUPS, 3, body)
                sp.wait_ge(stored, 16 * GROUPS)

            @block.gpsimd
            def _(pool):
                pool.memset(w1_f[:, :, :, HID:HPAD], 0.0).then_inc(w1_clear, 1)
                pool.memset(b1_in[:], 0.0).then_inc(w1_clear, 1)
                pool.memset(w2_f[:, KH - 1], 0.0).then_inc(w2_clear, 1)
                pool.memset(h_hi[:, :, KH - 1].bitcast(F32), 0.0).then_inc(h_pads, 1)
                pool.memset(h_lo[:, :, KH - 1].bitcast(F32), 0.0).then_inc(h_pads, 1)
                pool.wait_ge(h_pads, 2)
                pool.memset(h_hi[BIAS_ROW:BIAS_ROW + 1, :, KH - 1].bitcast(F32), 1.0).then_inc(h_pads, 1)

                def body(t, j, u, on):
                    if on(0):
                        need(pool, s["eps_done"], t + 1)
                        need(pool, s["norm"], 2 * GROUP * t)
                        pool.tensor_tensor(rstd[:], var[:], c["neg_half"][:, 0:GROUP], ALU.pow
                                           ).then_inc(s["rstd_done"], 1)

                run_steps(pool, GROUPS, 2, body)

            @block.scalar
            def _(act):
                act.wait_ge(b1_done, 1)
                act.wait_ge(h_pads, 3)

                def body(t, j, u, on):
                    for k in range(KH):
                        if on(1):
                            slot = (u - 1) % 2
                            n = KH * (t - 1) + k
                            rows_ = P if k < KH - 1 else HTAIL
                            need(act, s["h_ps"], n + 1)
                            need(act, s["gated_done"], n - 1)
                            act.activation(gate[:, k % 2], ps_h[:, k % 2, 1], ACT.Gelu, bias=b1_col[:, 1, k:k + 1]
                                           ).then_inc(s["gate_done"], 1)
                            need(act, s["gated_done"], n + 1)
                            need(act, s["out_ps"], GROUP * (t - 2))
                            act.activation(h_hi[0:rows_, slot, k], gated[0:rows_, k % 2], ACT.Copy
                                           ).then_inc(s["h_hi"], 1)
                        if on(0) and k == XT_AT:
                            for kk in range(KD):
                                need(act, s["xT_ps"], KD * t + kk + 1)
                                need(act, s["h_ps"], KH * (t - 1))
                                act.activation(xT_hi[:, u, kk], ps_T[:, kk], ACT.Copy).then_inc(s["xT_hi"], 1)

                run_steps(act, GROUPS, 2, body)

            @block.vector
            def _(dve):
                dve.wait_ge(w_ld, 16 * KD)
                dve.wait_ge(c_ld, 16 * 6)
                dve.wait_ge(b1_ps, 1)
                dve.tensor_tensor(b1_col[:].rearrange("p a k -> p (a k)"), b1_in[:].rearrange("p a k -> p (a k)"),
                                  ps_T[:, 0, 0:2 * KH], ALU.add).then_inc(b1_done, 1)
                for k in range(KD):
                    wk = w1_f[:, k].rearrange("p a n -> p (a n)")
                    dve.tensor_scalar(wk, wk, g_col[:, k:k + 1], None, ALU.mult).then_inc(w1_scaled, 1)
                    dve.wait_ge(w1_scaled, k + 1)
                    split(dve, w1_hi[:, k].rearrange("p a n -> p (a n)"), w1_lo[:, k].rearrange("p a n -> p (a n)"), wk,
                          w1_split, 2 * k)
                dve.wait_ge(w2_ld, 48)
                split(dve, w2_hi[:], w2_lo[:], w2_f[:], w2_split, 0)
                dve.wait_ge(h_pads, 3)

                def block_of(t, u, k):
                    n = KH * (t - 1) + k
                    need(dve, s["gate_done"], n + 1)
                    need(dve, s["h_lo"], n - 1)
                    dve.scalar_tensor_tensor(out=gated[:, k % 2], in0=ps_h[:, k % 2, 0], scalar=b1_col[:, 0, k:k + 1],
                                             in1=gate[:, k % 2], op0=ALU.add, op1=ALU.mult).then_inc(s["gated_done"], 1)

                def low_part(t, u, k):
                    slot, n = (u - 1) % 2, KH * (t - 1) + k
                    rows_ = P if k < KH - 1 else HTAIL
                    need(dve, s["h_hi"], n + 1)
                    dve.tensor_tensor(h_lo[0:rows_, slot, k], gated[0:rows_, k % 2], h_hi[0:rows_, slot, k].bitcast(F32),
                                      ALU.subtract).then_inc(s["h_lo"], 1)

                def row_done(t, r):
                    n = GROUP * (t - 2) + r
                    need(dve, s["out_ps"], n + 1)
                    if r == 0:
                        need(dve, res_ld, per_res * (t - 1))
                        need(dve, stored, 16 * (t - 2))
                    dst = x_new[:, r]
                    dve.tensor_tensor(dst, ps_out, x_res[:, r], ALU.add).then_inc(s["x_done"], 1)
                    if extra is not None:
                        need(dve, s["x_done"], n + 1)
                        dve.tensor_tensor(dst, dst, add[:, r], ALU.add).then_inc(s["sum_done"], 1)

                def statistics(t, j, u):
                    n = GROUP * t
                    need(dve, x_ld[u], 16 * (j + 1))
                    need(dve, s["norm"], 2 * n)
                    for r in range(GROUP):
                        dve.bn_stats(stats[:, r, 0], x[:, u, r, 0:P]).then_inc(s["stat"], 1)
                    need(dve, s["shift_ps"], t + 1)
                    for r in range(GROUP):
                        dve.bn_stats(stats[:, r, 1], ps_shift[:, r]).then_inc(s["stat"], 1)
                    need(dve, s["stat"], 2 * GROUP * (t + 1))
                    take_wait(dve, scratch[:])
                    for r in range(GROUP):
                        dve.bn_aggr(mv[:, r], stats[:, r]).then_inc(s["aggr"], 1)
                    need(dve, s["aggr"], n + GROUP)
                    dve.tensor_scalar(var[:], mv[:, :, 1], EPS, None, ALU.add).then_inc(s["eps_done"], 1)

                def normalise(t, u):
                    need(dve, s["rstd_done"], t + 1)
                    need(dve, s["xT_ps"], KD * t)
                    for r in range(GROUP):
                        for k, src in ((0, x[:, u, r, 0:P]), (1, ps_shift[:, r])):
                            dve.tensor_scalar(xn[:, r, k * P:(k + 1) * P], src, mv[:, r, 0:1], rstd[:, r:r + 1],
                                              ALU.subtract, ALU.mult).then_inc(s["norm"], 1)

                def body(t, j, u, on):
                    for k in range(KH):
                        if on(2) and 1 <= k <= GROUP:
                            row_done(t, k - 1)
                        if on(1):
                            block_of(t, u, k)
                            if k:
                                low_part(t, u, k - 1)
                        if on(0) and k == 0:
                            statistics(t, j, u)
                        if on(0) and k == 1:
                            normalise(t, u)
                        if on(0) and k == XT_AT:
                            for kk in range(KD):
                                need(dve, s["xT_hi"], KD * t + kk + 1)
                                dve.tensor_tensor(xT_lo[:, u, kk], ps_T[:, kk], xT_hi[:, u, kk].bitcast(F32),
                                                  ALU.subtract).then_inc(s["xT_lo"], 1)
                    if on(1):
                        low_part(t, u, KH - 1)

                run_steps(dve, GROUPS, 2, body)

            @block.tensor
            def _(pe):
                pe.wait_ge(w_ld, 16 * KD)
                pe.wait_ge(c_ld, 16 * 6)
                pe.wait_ge(w1_clear, 2)
                for a in range(2):
                    for n in range(KH):
                        for k in range(KD):
                            col = a * KH + n
                            last = pe.matmul(ps_T[:, 0, col:col + 1], w1_f[:, k, a, n * P:(n + 1) * P], b_col[:, k:k + 1],
                                             start=(k == 0), stop=(k == KD - 1))
                last.then_inc(b1_ps, 1)
                pe.wait_ge(b1_done, 1)
                pe.wait_ge(w1_split, 2 * KD)
                pe.wait_ge(w2_split, 2)

                def hidden(t, u, k):
                    slot, n = (u - 1) % 2, KH * (t - 1) + k
                    need(pe, s["gated_done"], n - 1)
                    if k == 0:
                        need(pe, s["xT_hi"], KD * t)
                        need(pe, s["xT_lo"], KD * t)
                    cols = slice(k * P, (k + 1) * P)
                    for a in (1, 0):
                        out = ps_h[:, k % 2, a]
                        for kk in range(KD):
                            pe.matmul(out, w1_hi[:, kk, a, cols], xT_hi[:, slot, kk], start=(kk == 0), stop=False)
                            pe.matmul(out, w1_hi[:, kk, a, cols], xT_lo[:, slot, kk], start=False, stop=False)
                            last = pe.matmul(out, w1_lo[:, kk, a, cols], xT_hi[:, slot, kk], start=False,
                                             stop=(kk == KD - 1))
                    last.then_inc(s["h_ps"], 1)

                def row_out(t, u, r):
                    n = GROUP * (t - 2) + r
                    slot = u
                    need(pe, s["x_done"], n)
                    if r == 0:
                        need(pe, s["h_lo"], KH * (t - 1))
                    tok = slice(r * P, (r + 1) * P)
                    for k in range(KH):
                        pe.matmul(ps_out, h_hi[:, slot, k, tok], w2_hi[:, k], start=(k == 0), stop=False)
                        pe.matmul(ps_out, h_hi[:, slot, k, tok], w2_lo[:, k], start=False, stop=False)
                        last = pe.matmul(ps_out, h_lo[:, slot, k, tok], w2_hi[:, k], start=False, stop=(k == KH - 1))
                    last.then_inc(s["out_ps"], 1)

                def body(t, j, u, on):
                    if on(0):
                        need(pe, x_ld[u], 16 * (j + 1))
                        need(pe, s["norm"], 2 * GROUP * t)
                        for r in range(GROUP):
                            last = pe.matmul(ps_shift[:, r], c["shift"][:], x[:, u, r, P:D], start=True, stop=True)
                        last.then_inc(s["shift_ps"], 1)
                    for k in range(KH):
                        if on(1):
                            hidden(t, u, k)
                        if on(2) and k < GROUP:
                            row_out(t, u, k)
                        if on(0) and k == XT_AT:
                            need(pe, s["norm"], 2 * GROUP * (t + 1))
                            need(pe, s["xT_lo"], KD * t)
                            for kk in range(KD):
                                for r in range(GROUP):
                                    last = pe.transpose(ps_T[:, kk, r * P:(r + 1) * P], xn[:, r, kk * P:(kk + 1) * P],
                                                        c["ident"][:])
                                last.then_inc(s["xT_ps"], 1)

                run_steps(pe, GROUPS, 2, body)
        m.end()


def min_int(n, bound):
    return min(n, bound) if isinstance(n, int) else n


_INS = ['x', 'L0_tok_W_h', 'L0_tok_b_h', 'L0_tok_W_o', 'L0_tok_b_o', 'L0_tok_W_r', 'L0_tok_b_r', 'L0_ffn_wqkv',
        'L0_ffn_q_scale', 'L0_ffn_k_scale', 'L0_ffn_wo', 'L0_ffn_ln_g', 'L0_ffn_ln_b', 'L0_ffn_w1', 'L0_ffn_b1',
        'L0_ffn_w2', 'L0_ffn_b2']


def rotary_tables():
    half_idx = np.arange(0, HD, 2, dtype=np.float32)
    inv_freq = (np.float32(1.0) / np.float32(10000.0) ** (half_idx / np.float32(HD))).astype(np.float32)
    t = np.arange(TOKENS, dtype=np.float32)
    freqs = t[:, None] * inv_freq[None, :]
    freqs = np.concatenate([freqs, freqs], axis=-1)
    base = (half_idx + np.float32(0.4 * HD)) / np.float32(1.4 * HD)
    power = (t - TOKENS // 2) / np.float32(64.0)
    scale = base[None, :] ** power[:, None]
    scale = np.concatenate([scale, scale], axis=-1)
    sign = np.concatenate([-np.ones(HD // 2), np.ones(HD // 2)]).astype(np.float32)
    cos, sin = np.cos(freqs), np.sin(freqs) * sign
    qk_scale = np.float32(8.0)
    return (np.stack([cos * scale * qk_scale, cos / scale], axis=1).astype(np.float32),
            np.stack([sin * scale * qk_scale, sin / scale], axis=1).astype(np.float32))


def audio_tower(nc, x, W_h, b_h, W_o, b_o, W_r, b_r, wqkv, q_scale, k_scale, wo, ln_g, ln_b, w1, b1, w2, b2,
                cos, sin, out):
    shape = (ROWS, TOKENS, D)
    h1, h2, xa, xb = [nc.dram_tensor(n, shape, F32, kind="Internal").ap() for n in ("h1", "h2", "xa", "xb")]
    with ExitStack() as ctx:
        c = constants(nc, Memory(nc, ctx, "const"))
        tokenizer(nc, c, x, W_h, b_h, W_o, b_o, W_r, b_r, h1)
        identity_attention(nc, c, h1, h2, xa)
        for layer in range(DEPTH):
            last = layer == DEPTH - 1
            layer_attention(nc, c, layer, wqkv, q_scale, k_scale, wo, cos, sin, xa, xb)
            layer_forward(nc, c, layer, ln_g, ln_b, w1, b1, w2, b2, xb, out if last else xa, h2 if last else None)


def kernel(**inputs):
    import concourse.bacc as bacc
    from concourse.bass_utils import run_bass_kernel_spmd

    nc = bacc.Bacc("TRN2", target_bir_lowering=False, num_devices=1)
    cos, sin = rotary_tables()
    arrays, args = {}, []
    for name, a in [(n, inputs[n]) for n in _INS] + [("rope_cos", cos), ("rope_sin", sin)]:
        a = np.ascontiguousarray(a)
        arrays[f"in_{name}"] = a
        args.append(nc.dram_tensor(f"in_{name}", a.shape, mybir.dt.from_np(a.dtype), kind="ExternalInput").ap())
    args.append(nc.dram_tensor("out", (ROWS, TOKENS, D), F32, kind="ExternalOutput").ap())
    audio_tower(nc, *args)
    r = run_bass_kernel_spmd(nc, [arrays], core_ids=[0])
    return r.results[0]["out"]
```
